# Optimizing a Trainium2 kernel written in Bass

```python
import numpy as np
import jax
import jax.numpy as jnp

def _softmax(x, axis=-1):
    return jax.nn.softmax(x, axis=axis)

def _gelu(x):
    return jax.nn.gelu(x, approximate=True)

def _silu(x):
    return jax.nn.silu(x)

def _sigmoid(x):
    return jax.nn.sigmoid(x)

def _layernorm(x, axis=-1, eps=1e-05):
    m = jnp.mean(x, axis=axis, keepdims=True)
    v = jnp.var(x, axis=axis, keepdims=True)
    return (x - m) / jnp.sqrt(v + eps)

def _scatter_add(tgt, idx, src, axis=0):
    return tgt.at[idx].add(src)

def _segment_sum(src, seg, n):
    return jax.ops.segment_sum(src, seg, n)
kernel_name = 'mk_xattn_seq_d1_seqx_r2_9019f8'

def setup_inputs(seed: int=0):
    np.random.seed(seed)
    _w = jnp.asarray

    def _rec_inputs():
        import jax
        import jax.numpy as jnp
        _rk = jax.random.key(seed)
        x = -0.0003929 + 0.9999 * jax.random.normal(jax.random.fold_in(_rk, 1), (8, 1024, 1024), jnp.float32)
        _lenS = 1024 - jax.random.randint(jax.random.fold_in(_rk, 7), (8,), 0, max(1, 1024 // 4) + 1, jnp.int32)
        _lenS2 = 64 - jax.random.randint(jax.random.fold_in(_rk, 8), (8,), 0, max(1, 64 // 4) + 1, jnp.int32)
        _ctx_2048P = jax.random.normal(jax.random.fold_in(_rk, 11), (8, 16, 1024), jnp.float32)
        _ctx_2048c = jax.random.dirichlet(jax.random.fold_in(_rk, 511), 0.3 * jnp.ones((16,), jnp.float32), (8, 64))
        _ctx_2048t = jnp.einsum('bsk,bkd->bsd', _ctx_2048c, _ctx_2048P)
        _ctx_2048t = _ctx_2048t * jax.lax.rsqrt(jnp.mean(jnp.square(_ctx_2048t)) + 1e-12) * 0.953939
        ctx_2048 = -8.57375e-05 + 0.999917 * (_ctx_2048t + 0.3 * jax.random.normal(jax.random.fold_in(_rk, 611), (8, 64, 1024), jnp.float32))
        _validS = jnp.arange(1024)[None, :] < _lenS[:, None]
        _validS2 = jnp.arange(64)[None, :] < _lenS2[:, None]
        _causal = jnp.tril(jnp.ones((1024, 1024), dtype=bool))
        mask_BxS2_bf1 = jnp.ones((8, 64), dtype=bool)
        return (x, ctx_2048, mask_BxS2_bf1)
    x, ctx_2048, mask_BxS2_bf1 = _rec_inputs()

    def _L0_xattn_setup():
        import jax, jax.numpy as jnp
        import numpy as np
        HIDDEN = 1024
        HEADS = 16
        HEAD_DIM = HIDDEN // HEADS
        LN_EPS = 1e-05
        GATE_INIT = 0.5

        def _layer_norm(x, gamma, beta):
            mu = jnp.mean(x, axis=-1, keepdims=True)
            var = jnp.mean(jnp.square(x - mu), axis=-1, keepdims=True)
            return (x - mu) * jax.lax.rsqrt(var + LN_EPS) * gamma + beta
        key = jax.random.key(seed)
        ks = jax.random.split(key, 8)
        B, T_TEXT, T_AUDIO = (4, 1024, 750)
        s = 0.02
        return {'hidden_states': jax.random.normal(ks[0], (B, T_TEXT, HIDDEN), jnp.float32), 'audio_kv': jax.random.normal(ks[1], (B, T_AUDIO, HIDDEN), jnp.float32), 'audio_attention_mask': jnp.ones((B, T_AUDIO), dtype=bool), 'Wq': jax.random.normal(ks[2], (HIDDEN, HIDDEN), jnp.float32) * s, 'Wk': jax.random.normal(ks[3], (HIDDEN, HIDDEN), jnp.float32) * s, 'Wv': jax.random.normal(ks[4], (HIDDEN, HIDDEN), jnp.float32) * s, 'Wo': jax.random.normal(ks[5], (HIDDEN, HIDDEN), jnp.float32) * s, 'ln_gamma': jnp.ones((HIDDEN,), jnp.float32), 'ln_beta': jnp.zeros((HIDDEN,), jnp.float32), 'gate': jnp.array([GATE_INIT], jnp.float32)}
    _L0_xattn_all = _L0_xattn_setup()
    _L0_xattn_in = {k: v for k, v in _L0_xattn_all.items() if k in ('Wq', 'Wk', 'Wv', 'Wo', 'ln_gamma', 'ln_beta', 'gate')}
    del _L0_xattn_all
    return {'x': x, 'ctx_2048': ctx_2048, 'mask_BxS2_bf1': mask_BxS2_bf1, 'L0_xattn_Wq': _L0_xattn_in['Wq'], 'L0_xattn_Wk': _L0_xattn_in['Wk'], 'L0_xattn_Wv': _L0_xattn_in['Wv'], 'L0_xattn_Wo': _L0_xattn_in['Wo'], 'L0_xattn_ln_gamma': _L0_xattn_in['ln_gamma'], 'L0_xattn_ln_beta': _L0_xattn_in['ln_beta'], 'L0_xattn_gate': _L0_xattn_in['gate']}

def reference(x, ctx_2048, mask_BxS2_bf1, L0_xattn_Wq, L0_xattn_Wk, L0_xattn_Wv, L0_xattn_Wo, L0_xattn_ln_gamma, L0_xattn_ln_beta, L0_xattn_gate):
    import jax
    import jax.numpy as jnp

    def _L0_xattn_ref(hidden_states, audio_kv, audio_attention_mask, Wq, Wk, Wv, Wo, ln_gamma, ln_beta, gate):
        import jax, jax.numpy as jnp
        import numpy as np
        HIDDEN = 1024
        HEADS = 16
        HEAD_DIM = HIDDEN // HEADS
        LN_EPS = 1e-05
        GATE_INIT = 0.5

        def _layer_norm(x, gamma, beta):
            mu = jnp.mean(x, axis=-1, keepdims=True)
            var = jnp.mean(jnp.square(x - mu), axis=-1, keepdims=True)
            return (x - mu) * jax.lax.rsqrt(var + LN_EPS) * gamma + beta
        B, Tt, D = hidden_states.shape
        Ta = audio_kv.shape[1]
        scale = HEAD_DIM ** (-0.5)
        a = _layer_norm(audio_kv, ln_gamma, ln_beta)
        Q = (hidden_states @ Wq.T).reshape(B, Tt, HEADS, HEAD_DIM).transpose(0, 2, 1, 3)
        K = (a @ Wk.T).reshape(B, Ta, HEADS, HEAD_DIM).transpose(0, 2, 1, 3)
        V = (a @ Wv.T).reshape(B, Ta, HEADS, HEAD_DIM).transpose(0, 2, 1, 3)
        scores = jnp.einsum('bhtd,bhsd->bhts', Q, K) * scale
        mask = audio_attention_mask[:, None, None, :]
        scores = jnp.where(mask, scores, jnp.float32(-jnp.inf))
        attn = jax.nn.softmax(scores, axis=-1)
        out = jnp.einsum('bhts,bhsd->bhtd', attn, V)
        out = out.transpose(0, 2, 1, 3).reshape(B, Tt, D)
        out = out @ Wo.T
        return hidden_states + jnp.tanh(gate) * out
    x = _L0_xattn_ref(x, ctx_2048, mask_BxS2_bf1, L0_xattn_Wq, L0_xattn_Wk, L0_xattn_Wv, L0_xattn_Wo, L0_xattn_ln_gamma, L0_xattn_ln_beta, L0_xattn_gate)
    return x

_drawn_inputs = setup_inputs


def setup_inputs(seed=0):
    import zlib

    import numpy as np

    out = dict(_drawn_inputs(seed))
    spreads = {'L0_xattn_ln_gamma': (1.0, 0.6), 'L0_xattn_ln_beta': (0.0, 0.428)}
    factors = {'L0_xattn_Wq': 3.727, 'L0_xattn_Wk': 3.745}
    for name, (base, spread) in spreads.items():
        noise = np.random.default_rng([zlib.crc32(name.encode()), seed]).standard_normal(out[name].shape)
        drawn = base * np.exp(spread * noise) if base else spread * noise
        out[name] = jnp.asarray(drawn.astype(out[name].dtype))
    for name, factor in factors.items():
        out[name] = (out[name] * factor).astype(out[name].dtype)
    return out
```

```python
from contextlib import ExitStack

import concourse.bass as bass
from concourse import mybir

ALU = mybir.AluOpType
ACT = mybir.ActivationFunctionType
AX = mybir.AxisListType
F32 = mybir.dt.float32
F32R = mybir.dt.float32r
U8 = mybir.dt.uint8

P = 128
EPS = 1e-5
HEAD = 64


def xattn_kernel(nc, x, x_t, ctx_x, mask, wq_t, wk_t, wv_t, wo_t, gamma, beta, gate, out):
    rows, D = x.shape
    B, S = mask.shape
    T = rows // B
    TB = 512
    NBLK = T // TB
    NC = D // P
    UNITS = NBLK * NC
    TILES = T // P
    TPB = TB // P
    CT = B * S // P
    G = NC // 2
    GROUPS = TPB * 2
    WSLOTS = 4
    SCORES_LAG, TRANSPOSE_LAG, VALUES_LAG, STORE_LAG = 1, 2, 3, 4
    assert NBLK == 2 and NC == 8 and CT == 4 and B * S == TB

    k_scr = nc.dram_tensor("k_scratch", [P, NC, B * S], F32, kind="Internal").ap()
    vhi_scr = nc.dram_tensor("v_hi_scratch", [B * S, D], F32, kind="Internal").ap()
    vlo_scr = nc.dram_tensor("v_lo_scratch", [B * S, D], F32, kind="Internal").ap()
    ot_scr = nc.dram_tensor("o_t_scratch", [B * D, T], F32, kind="Internal").ap()

    with ExitStack() as ctx:
        def sb(name, shape, dt=F32):
            return ctx.enter_context(nc.sbuf_tensor(name, shape, dt))

        def sem(name):
            return ctx.enter_context(nc.semaphore(name))

        def sems(name, n):
            return [sem(f"{name}{i}") for i in range(n)]

        banks = ctx.enter_context(nc.psum_tensor("banks", [P, 8, 512], F32))

        w_hi = sb("w_hi", [P, NC, D], F32R)
        w_lo = sb("w_lo", [P, NC, D], F32R)
        act_in = sb("act_in", [P, NC, TB])
        act_hi = sb("act_hi", [P, 2, NC, TB], F32R)
        act_lo = sb("act_lo", [P, 2, NC, TB], F32R)
        w_stage = sb("w_stage", [P, WSLOTS, D])
        k_diag = sb("k_diag", [P, NC, P])
        v_diag_hi = sb("v_diag_hi", [P, NC, P], F32R)
        v_diag_lo = sb("v_diag_lo", [P, NC, P], F32R)
        q_t = sb("q_t", [P, 2, TB])
        probs = sb("probs", [P, 4, TB])
        p_hi = sb("p_hi", [P, 2, TB], F32R)
        p_lo = sb("p_lo", [P, 2, TB], F32R)
        o_t = sb("o_t", [P, 2, TB])
        ident = sb("ident", [P, P])
        mask_u8 = sb("mask_u8", [P, B, S], U8)
        mask_bias = sb("mask_bias", [P, B, S])
        gamma_s = sb("gamma_s", [P, NC])
        beta_s = sb("beta_s", [P, NC])
        gate_s = sb("gate_s", [P, 1])
        tanh_gate = sb("tanh_gate", [P, 1])
        neg_half = sb("neg_half", [P, 1])
        stats = sb("stats", [P, CT, 2, 6])
        mean_var = sb("mean_var", [P, CT, 2])
        var_eps = sb("var_eps", [P, CT])
        rstd = sb("rstd", [P, CT])
        neg_max = sb("neg_max", [P, 2, GROUPS])
        row_sum = sb("row_sum", [P, 2, GROUPS])
        row_rec = sb("row_rec", [P, 2, GROUPS])

        ctx_n = act_in[:].rearrange("p c t -> p (c t)").rearrange("p (i d) -> p i d", i=CT)
        a_hi, a_lo = act_hi[:, 1], act_lo[:, 1]
        ring_hi = act_hi[:, 0].rearrange("p c t -> p (c t)").rearrange("p (s d) -> p s d", s=WSLOTS)
        ring_lo = act_lo[:, 0].rearrange("p c t -> p (c t)").rearrange("p (s d) -> p s d", s=WSLOTS)
        out_hi = p_hi
        out_lo = p_lo
        res = [probs[:, 0:2, :], probs[:, 2:4, :], q_t[:, :, :], o_t[:, :, :]]

        consts_in = sem("consts_in")
        ident_zero = sem("ident_zero")
        ident_made = sem("ident_made")
        diag_zeroed = sem("diag_zeroed")
        mask_step = sem("mask_step")
        gate_ready = sem("gate_ready")
        ctx_in = sems("ctx_in", CT)
        stats_made = sem("stats_made")
        mean_made = sem("mean_made")
        var_added = sem("var_added")
        rstd_made = sem("rstd_made")
        normed = sem("normed")
        a_transposed = sem("a_transposed")
        a_scaled = sem("a_scaled")
        a_hi_made = sem("a_hi_made")
        a_lo_made = sem("a_lo_made")
        w_in = sems("w_in", WSLOTS)
        w_hi_made = sem("w_hi_made")
        w_lo_made = sem("w_lo_made")
        w_used = sem("w_used")
        k_copied = sem("k_copied")
        k_stored = sems("k_stored", 4)
        v_hi_copied = sem("v_hi_copied")
        v_lo_copied = sem("v_lo_copied")
        v_stored = sems("v_stored", 2)
        k_in = sems("k_in", G)
        v_in = sems("v_in", G)
        act_loaded = sems("act_loaded", NC)
        act_hi_made = sem("act_hi_made")
        act_lo_made = sem("act_lo_made")
        q_done = sem("q_done")
        q_copied = sem("q_copied")
        scores_done = sem("scores_done")
        masked = sem("masked")
        max_done = sem("max_done")
        shifted = sem("shifted")
        exp_done = sem("exp_done")
        sum_done = sem("sum_done")
        rec_done = sem("rec_done")
        probs_done = sem("probs_done")
        p_transposed = sem("p_transposed")
        p_hi_made = sem("p_hi_made")
        p_lo_made = sem("p_lo_made")
        o_done = sem("o_done")
        o_copied = sem("o_copied")
        o_stored = sems("o_stored", 2)
        res_in = sems("res_in", 4)
        out_done = sem("out_done")
        out_added = sem("out_added")
        out_stored = sems("out_stored", 4)

        def wait(eng, s, value):
            if not isinstance(value, int) or value > 0:
                eng.wait_ge(s, value)

        def steps(b, lags):
            for j in range(UNITS):
                for stage, lag in lags:
                    ju = j - lag
                    if ju >= 0:
                        stage(b, ju)
                    elif not isinstance(b, int) or b > 0:
                        stage(b - 1, ju + UNITS)

        def last_steps(lags):
            for j in range(max(lag for _, lag in lags)):
                for stage, lag in lags:
                    if j < lag:
                        stage(B - 1, j - lag + UNITS)

        def all_batches(eng, lags):
            steps(0, lags)
            with eng.Fori(1, B - 1) as b:
                steps(b, lags)
            steps(B - 1, lags)
            last_steps(lags)

        def weight_chunk(w):
            c = w % NC
            return (wk_t, wv_t, wq_t, wo_t)[w // NC][c * P:(c + 1) * P, :]

        def split_target(w):
            if w < 2 * NC:
                return ring_hi[:, w % WSLOTS, :], ring_lo[:, w % WSLOTS, :]
            return w_hi[:, w % NC, :], w_lo[:, w % NC, :]

        block = ctx.enter_context(nc.Block())

        @block.sync
        def _(sp):
            def load_weight(w):
                wait(sp, w_lo_made, w - WSLOTS + 1)
                sp.dma_start(w_stage[:, w % WSLOTS, :], weight_chunk(w)).then_inc(w_in[w % WSLOTS], 16)

            def load_act(b, blk, c, src):
                sp.dma_start(act_in[:, c, :], src[bass.ds(b * D + c * P, P), blk * TB:(blk + 1) * TB]
                             ).then_inc(act_loaded[c], 16)

            def load_k(b, q):
                for h in range(2):
                    r = slice(h * HEAD, (h + 1) * HEAD)
                    sp.dma_start(k_diag[r, 2 * q:2 * q + 2, r],
                                 k_scr[r, 2 * q:2 * q + 2, bass.ds(b * S, S)]).then_inc(k_in[q], 16)

            def load_v(b, q):
                for h in range(2):
                    r = slice(h * HEAD, (h + 1) * HEAD)
                    for diag, scr in ((v_diag_hi, vhi_scr), (v_diag_lo, vlo_scr)):
                        src = scr[bass.ds(b * S, S), 2 * q * P:(2 * q + 2) * P].rearrange(
                            "s (g e) -> s g e", g=2)[:, :, r]
                        sp.dma_start(diag[r, 2 * q:2 * q + 2, r].bitcast(F32), src).then_inc(v_in[q], 16)

            for i in range(CT):
                sp.dma_start(ctx_n[:, i, :], ctx_x[i * P:(i + 1) * P, :]).then_inc(ctx_in[i], 16)
            sp.dma_start(gamma_s[:], gamma).then_inc(consts_in, 16)
            sp.dma_start(beta_s[:], beta).then_inc(consts_in, 16)
            sp.dma_start(gate_s[:], gate.partition_broadcast(P)).then_inc(consts_in, 16)
            sp.dma_start(mask_u8[:], mask.partition_broadcast(P)).then_inc(consts_in, 16)
            for w in range(12):
                load_weight(w)
            for p in range(NC):
                sp.wait_ge(k_copied, p + 1)
                sp.dma_start(k_scr[:, p, :], probs[:, p % 4, :]).then_inc(k_stored[p % 4], 16)
            for w in range(12, 16):
                load_weight(w)
            sp.wait_ge(a_transposed, NC)
            for c in range(NC):
                load_act(0, 0, c, x_t)
            for w in range(16, 24):
                load_weight(w)
            for s in k_stored:
                sp.wait_ge(s, 32)
            sp.wait_ge(diag_zeroed, 3)
            for q in range(G):
                load_k(0, q)
            for i in range(2 * CT):
                sp.wait_ge(v_lo_copied, i + 1)
                r, cols = slice(i // 2 * P, (i // 2 + 1) * P), slice(i % 2 * 512, (i % 2 + 1) * 512)
                sp.dma_start(vhi_scr[r, cols], out_hi[:, i % 2, :].bitcast(F32)).then_inc(v_stored[i % 2], 16)
                sp.dma_start(vlo_scr[r, cols], out_lo[:, i % 2, :].bitcast(F32)).then_inc(v_stored[i % 2], 16)
            for s in v_stored:
                sp.wait_ge(s, 32 * CT)
            for q in range(G):
                load_v(0, q)
            for c in range(NC):
                sp.wait_ge(act_lo_made, c + 1)
                load_act(0, 1, c, x_t)
            for w in range(24, 24 + WSLOTS):
                load_weight(w)

            def store_o(b, j):
                u = b * UNITS + j
                sp.wait_ge(o_copied, u + 1)
                sp.dma_start(ot_scr[bass.ds(b * D + j % NC * P, P), j // NC * TB:(j // NC + 1) * TB],
                             o_t[:, j % 2, :]).then_inc(o_stored[j % 2], 16)

            def load_next_kv(b, j):
                if j < NC or j % 2 == 0 or (isinstance(b, int) and b == B - 1):
                    return
                sp.wait_ge(o_done, b * UNITS + j + 1)
                load_k(b + 1, (j - NC) // 2)
                load_v(b + 1, (j - NC) // 2)

            def load_block_after_next(b, j):
                blk, c = j // NC, j % NC
                sp.wait_ge(act_lo_made, (b * NBLK + blk + 1) * NC + c + 1)
                if isinstance(b, int) and b == B - 1:
                    sp.wait_ge(o_stored[c % 2], 16 * ((blk * NC + c) // 2 + 1))
                    load_act(0, blk, c, ot_scr)
                else:
                    load_act(b + 1, blk, c, x_t)

            all_batches(sp, [(load_block_after_next, 0), (store_o, STORE_LAG), (load_next_kv, STORE_LAG)])

            for w in range(24 + WSLOTS, 32):
                load_weight(w)
            for s in o_stored:
                sp.wait_ge(s, 16 * B * UNITS // 2)

            def load_res(b, j):
                v = b * TILES + j
                if isinstance(b, int) and b == 0 and j < 4:
                    sp.wait_ge(p_transposed, B * UNITS)
                else:
                    sp.wait_ge(out_stored[j % 4], 16 * (b * (TILES // 4) + j // 4))
                sp.dma_start(res[j % 4], x[bass.ds(v * P, P), :].rearrange("p (a n) -> p a n", a=2)
                             ).then_inc(res_in[j % 4], 16)

            def load_out_block(b, j):
                blk = j // TPB
                if isinstance(b, int) and b == B - 1:
                    return
                for c in (2 * (j % TPB), 2 * (j % TPB) + 1):
                    sp.wait_ge(act_lo_made, ((B + b) * NBLK + blk + 1) * NC + c + 1)
                    load_act(b + 1, blk, c, ot_scr)

            def store_out(b, j):
                v = b * TILES + j
                sp.wait_ge(out_added, v + 1)
                sp.dma_start(out[bass.ds(v * P, P), :].rearrange("p (a n) -> p a n", a=2), res[j % 4]
                             ).then_inc(out_stored[j % 4], 16)

            def out_batch(b):
                last = isinstance(b, int) and b == B - 1
                for j in range(TILES):
                    if j + 2 < TILES:
                        load_res(b, j + 2)
                    elif not last:
                        load_res(b + 1, j + 2 - TILES)
                    load_out_block(b, j)
                    store_out(b, j)

            load_res(0, 0)
            load_res(0, 1)
            out_batch(0)
            with sp.Fori(1, B - 1) as b:
                out_batch(b)
            out_batch(B - 1)
            for s in out_stored:
                sp.wait_ge(s, 16 * B * TILES // 4)

        @block.gpsimd
        def _(pool):
            nc.gpsimd.memset(ident[:], 0.0).then_inc(ident_zero, 1)
            pool.wait_ge(ident_zero, 1)
            nc.gpsimd.affine_select(out=ident[:], in_=ident[:], compare_op=ALU.not_equal, fill=1.0, base=0,
                                    pattern=[[-1, P]], channel_multiplier=1).then_inc(ident_made, 1)
            nc.gpsimd.memset(neg_half[:], -0.5).then_inc(ident_zero, 1)
            nc.gpsimd.memset(k_diag[:], 0.0).then_inc(diag_zeroed, 1)
            nc.gpsimd.memset(v_diag_hi[:].bitcast(F32), 0.0).then_inc(diag_zeroed, 1)
            nc.gpsimd.memset(v_diag_lo[:].bitcast(F32), 0.0).then_inc(diag_zeroed, 1)
            pool.wait_ge(ident_zero, 2)
            for i in range(CT):
                pool.wait_ge(var_added, i + 1)
                nc.gpsimd.tensor_tensor(rstd[:, i:i + 1], var_eps[:, i:i + 1], neg_half[:], ALU.pow
                                        ).then_inc(rstd_made, 1)

            def split_lo(n, par, c):
                pool.wait_ge(act_hi_made, n * NC + c + 1)
                nc.gpsimd.tensor_tensor(act_lo[:, par, c, :], act_in[:, c, :], act_hi[:, par, c, :].bitcast(F32),
                                        ALU.subtract).then_inc(act_lo_made, 1)

            for c in range(NC):
                split_lo(0, 0, c)

            def normalise(b, j):
                u = b * UNITS + j
                pr = probs[:, j % 4, :].rearrange("p (g s) -> p g s", s=S)
                rec = row_rec[:, j % 2, :].unsqueeze(2).to_broadcast([P, GROUPS, S])
                pool.wait_ge(rec_done, u + 1)
                nc.gpsimd.tensor_tensor(pr, pr, rec, ALU.mult).then_inc(probs_done, 1)

            def split_next(b, j):
                split_lo(b * NBLK + j // NC + 1, (j // NC + 1) % 2, j % NC)

            all_batches(pool, [(split_next, 0), (normalise, TRANSPOSE_LAG)])

            def out_batch(b):
                for j in range(TILES):
                    blk = j // TPB
                    if isinstance(b, int) and b == B - 1 and blk == 1:
                        continue
                    for c in (2 * (j % TPB), 2 * (j % TPB) + 1):
                        split_lo((B + b) * NBLK + blk + 1, (blk + 1) % 2, c)

            with pool.Fori(0, B - 1) as b:
                out_batch(b)
            out_batch(B - 1)

        @block.scalar
        def _(act):
            def split_weight_hi(w):
                act.wait_ge(w_in[w % WSLOTS], 16 * (w // WSLOTS + 1))
                if w < 2 * NC:
                    wait(act, w_used, w - WSLOTS + 1)
                nc.scalar.copy(split_target(w)[0], w_stage[:, w % WSLOTS, :]).then_inc(w_hi_made, 1)

            def split_hi(n, par, c):
                nc.scalar.copy(act_hi[:, par, c, :], act_in[:, c, :]).then_inc(act_hi_made, 1)

            act.wait_ge(consts_in, 64)
            nc.scalar.activation(tanh_gate[:], gate_s[:], ACT.Tanh).then_inc(gate_ready, 1)
            for w in range(WSLOTS):
                split_weight_hi(w)
            for c in range(NC):
                act.wait_ge(a_scaled, c + 1)
                nc.scalar.copy(a_hi[:, c, :], q_t[:, c % 2, :]).then_inc(a_hi_made, 1)
            for w in range(WSLOTS, NC):
                split_weight_hi(w)
            split_weight_hi(NC)
            split_weight_hi(NC + 1)
            for p in range(NC):
                act.wait_ge(w_used, NC)
                if p >= 4:
                    act.wait_ge(k_stored[p % 4], 16)
                nc.scalar.mul(probs[:, p % 4, :], banks[:, p, :], HEAD ** -0.5).then_inc(k_copied, 1)
            for w in range(NC + 2, 24):
                split_weight_hi(w)
            for c in range(NC):
                act.wait_ge(act_loaded[c], 16)
                act.wait_ge(w_used, 13 + c // 2)
                split_hi(0, 0, c)
            for i in range(2 * CT):
                act.wait_ge(w_used, 2 * NC)
                if i >= 2:
                    act.wait_ge(v_stored[i % 2], 32 * (i // 2))
                nc.scalar.copy(out_hi[:, i % 2, :], banks[:, i, :]).then_inc(v_hi_copied, 1)

            def copy_q(b, j):
                u = b * UNITS + j
                act.wait_ge(q_done, u + 1)
                wait(act, scores_done, u - 1)
                nc.scalar.copy(q_t[:, j % 2, :], banks[:, j % 2, :]).then_inc(q_copied, 1)

            def split_next(b, j):
                n = b * NBLK + j // NC
                act.wait_ge(act_loaded[j % NC], 16 * (n + 2))
                if j % NC == 0:
                    if isinstance(b, int) and b == 0 and j == 0:
                        act.wait_ge(w_used, 2 * NC)
                    else:
                        act.wait_ge(q_done, n * NC)
                split_hi(n + 1, (j // NC + 1) % 2, j % NC)

            def exponential(b, j):
                u = b * UNITS + j
                act.wait_ge(shifted, u + 1)
                nc.scalar.activation(probs[:, j % 4, :], probs[:, j % 4, :], ACT.Exp).then_inc(exp_done, 1)

            def split_p_hi(b, j):
                u = b * UNITS + j
                act.wait_ge(p_transposed, u + 1)
                wait(act, o_done, u - 1)
                if isinstance(b, int) and b == 0 and j < 2:
                    act.wait_ge(v_stored[j], 32 * CT)
                nc.scalar.copy(p_hi[:, j % 2, :], banks[:, 4 + j % 2, :]).then_inc(p_hi_made, 1)

            def copy_o(b, j):
                u = b * UNITS + j
                act.wait_ge(o_done, u + 1)
                wait(act, o_stored[j % 2], b * (16 * UNITS // 2) + 16 * (j // 2))
                nc.scalar.copy(o_t[:, j % 2, :], banks[:, 6 + j % 2, :]).then_inc(o_copied, 1)

            all_batches(act, [(copy_q, 1), (split_p_hi, VALUES_LAG), (split_next, 0),
                              (copy_o, STORE_LAG), (exponential, SCORES_LAG)])

            act.wait_ge(q_done, B * UNITS)
            for w in range(24, 32):
                split_weight_hi(w)

            def out_batch(b):
                for j in range(TILES):
                    blk = j // TPB
                    if isinstance(b, int) and b == B - 1 and blk == 1:
                        continue
                    n = (B + b) * NBLK + blk
                    for c in (2 * (j % TPB), 2 * (j % TPB) + 1):
                        act.wait_ge(act_loaded[c], 16 * (n + 2))
                        if c == 0:
                            if isinstance(b, int) and b == 0 and j == 0:
                                act.wait_ge(q_done, B * UNITS)
                            else:
                                act.wait_ge(out_done, (b * NBLK + blk) * TPB)
                        split_hi(n + 1, (blk + 1) % 2, c)

            out_batch(0)
            with act.Fori(1, B - 1) as b:
                out_batch(b)
            out_batch(B - 1)

        @block.vector
        def _(dve):
            dve.wait_ge(consts_in, 64)
            bias_flat, mask_flat = mask_bias[:], mask_u8[:]
            nc.vector.tensor_scalar(bias_flat, mask_flat, -1.0, 3e38, ALU.add, ALU.mult).then_inc(mask_step, 1)
            dve.wait_ge(mask_step, 1)
            nc.vector.tensor_scalar(bias_flat, bias_flat, 3e38, None, ALU.mult).then_inc(mask_step, 1)

            for i in range(CT):
                dve.wait_ge(ctx_in[i], 16)
                for h in range(2):
                    nc.vector.bn_stats(stats[:, i, h, :], ctx_n[:, i, h * 512:(h + 1) * 512]).then_inc(stats_made, 1)
                dve.wait_ge(stats_made, 2 * i + 2)
                nc.vector.bn_aggr(mean_var[:, i, :], stats[:, i, :, :]).then_inc(mean_made, 1)
                dve.wait_ge(mean_made, i + 1)
                nc.vector.tensor_scalar(var_eps[:, i:i + 1], mean_var[:, i, 1:2], EPS, None, ALU.add
                                        ).then_inc(var_added, 1)
            for i in range(CT):
                dve.wait_ge(rstd_made, i + 1)
                nc.vector.tensor_scalar(ctx_n[:, i, :], ctx_n[:, i, :], mean_var[:, i, 0:1], rstd[:, i:i + 1],
                                        ALU.subtract, ALU.mult).then_inc(normed, 1)

            def split_weight_lo(w):
                hi, lo = split_target(w)
                dve.wait_ge(w_hi_made, w + 1)
                nc.vector.tensor_tensor(lo, w_stage[:, w % WSLOTS, :], hi.bitcast(F32), ALU.subtract
                                        ).then_inc(w_lo_made, 1)

            for w in range(WSLOTS):
                split_weight_lo(w)
            for c in range(NC):
                dve.wait_ge(a_transposed, c + 1)
                if c >= 2:
                    dve.wait_ge(a_lo_made, c - 1)
                nc.vector.tensor_scalar(q_t[:, c % 2, :], banks[:, c, :], gamma_s[:, c:c + 1], beta_s[:, c:c + 1],
                                        ALU.mult, ALU.add).then_inc(a_scaled, 1)
                dve.wait_ge(a_hi_made, c + 1)
                nc.vector.tensor_tensor(a_lo[:, c, :], q_t[:, c % 2, :], a_hi[:, c, :].bitcast(F32), ALU.subtract
                                        ).then_inc(a_lo_made, 1)
            for w in range(WSLOTS, 24):
                split_weight_lo(w)
            for i in range(2 * CT):
                dve.wait_ge(v_hi_copied, i + 1)
                nc.vector.tensor_tensor(out_lo[:, i % 2, :], banks[:, i, :], out_hi[:, i % 2, :].bitcast(F32),
                                        ALU.subtract).then_inc(v_lo_copied, 1)

            def split_p_lo(b, j):
                u = b * UNITS + j
                dve.wait_ge(p_hi_made, u + 1)
                nc.vector.tensor_tensor(p_lo[:, j % 2, :], banks[:, 4 + j % 2, :], p_hi[:, j % 2, :].bitcast(F32),
                                        ALU.subtract).then_inc(p_lo_made, 1)

            def grouped(j):
                return probs[:, j % 4, :].rearrange("p (g s) -> p g s", s=S)

            def sum_rows(b, j):
                u = b * UNITS + j
                dve.wait_ge(exp_done, u + 1)
                nc.vector.reduce_sum(row_sum[:, j % 2, :], grouped(j), AX.X).then_inc(sum_done, 1)

            def invert_sums(b, j):
                u = b * UNITS + j
                dve.wait_ge(sum_done, u + 1)
                wait(dve, probs_done, u - 1)
                nc.vector.reciprocal(row_rec[:, j % 2, :], row_sum[:, j % 2, :]).then_inc(rec_done, 1)

            def mask_scores(b, j):
                u = b * UNITS + j
                dve.wait_ge(scores_done, u + 1)
                wait(dve, p_transposed, u - 3)
                if isinstance(b, int) and b == 0 and j < 4:
                    dve.wait_ge(k_stored[j], 32)
                bias = mask_bias[:, bass.ds(b, 1), :].to_broadcast([P, GROUPS, S])
                scores = banks[:, 2 + j % 2, :].rearrange("p (g s) -> p g s", s=S)
                nc.vector.tensor_tensor(grouped(j), scores, bias, ALU.add).then_inc(masked, 1)

            def row_max(b, j):
                u = b * UNITS + j
                dve.wait_ge(masked, u + 1)
                nc.vector.tensor_reduce(neg_max[:, j % 2, :], grouped(j), AX.X, ALU.max, negate=True
                                        ).then_inc(max_done, 1)

            def shift(b, j):
                u = b * UNITS + j
                dve.wait_ge(max_done, u + 1)
                top = neg_max[:, j % 2, :].unsqueeze(2).to_broadcast([P, GROUPS, S])
                nc.vector.tensor_tensor(grouped(j), grouped(j), top, ALU.add).then_inc(shifted, 1)

            all_batches(dve, [(sum_rows, TRANSPOSE_LAG), (split_p_lo, VALUES_LAG), (invert_sums, TRANSPOSE_LAG),
                              (mask_scores, SCORES_LAG), (row_max, SCORES_LAG), (shift, SCORES_LAG)])

            for w in range(24, 32):
                split_weight_lo(w)

            def out_batch(b):
                for j in range(TILES):
                    v = b * TILES + j
                    if isinstance(b, int) and b == 0 and j == 0:
                        dve.wait_ge(gate_ready, 1)
                    dve.wait_ge(out_done, v + 1)
                    dve.wait_ge(res_in[j % 4], 16 * (b * (TILES // 4) + j // 4 + 1))
                    k = 2 * (j % 4)
                    nc.vector.scalar_tensor_tensor(out=res[j % 4], in0=banks[:, k:k + 2, :], scalar=tanh_gate[:, 0:1],
                                                   in1=res[j % 4], op0=ALU.mult, op1=ALU.add).then_inc(out_added, 1)

            out_batch(0)
            with dve.Fori(1, B - 1) as b:
                out_batch(b)
            out_batch(B - 1)

        @block.tensor
        def _(pe):
            def product(to, w_parts, m_parts, first, last):
                (wh, wl), (mh, ml) = w_parts, m_parts
                pe.matmul(to, wl, mh, start=first, stop=False)
                pe.matmul(to, wh, ml, start=False, stop=False)
                return pe.matmul(to, wh, mh, start=False, stop=last)

            pe.wait_ge(ident_made, 1)
            for i in range(CT):
                pe.wait_ge(normed, i + 1)
                for c in range(NC):
                    t = pe.transpose(banks[:, c, i * P:(i + 1) * P], ctx_n[:, i, c * P:(c + 1) * P], ident[:])
                    if i == CT - 1:
                        t.then_inc(a_transposed, 1)

            for c in range(NC):
                pe.wait_ge(w_lo_made, c + 1)
                pe.wait_ge(a_lo_made, c + 1)
                if c == 0:
                    pe.wait_ge(a_scaled, NC)
                for p in range(NC):
                    cols = slice(p * P, (p + 1) * P)
                    m = product(banks[:, p, :],
                                (ring_hi[:, c % WSLOTS, cols], ring_lo[:, c % WSLOTS, cols]),
                                (a_hi[:, c, :], a_lo[:, c, :]), c == 0, c == NC - 1)
                m.then_inc(w_used, 1)
            for c in range(NC):
                w = NC + c
                pe.wait_ge(w_lo_made, w + 1)
                for i in range(2 * CT):
                    if c == 0:
                        pe.wait_ge(k_copied, i + 1)
                    rows_, cols = slice(i // 2 * P, (i // 2 + 1) * P), slice(i % 2 * 512, (i % 2 + 1) * 512)
                    m = product(banks[:, i, :], (a_hi[:, c, rows_], a_lo[:, c, rows_]),
                                (ring_hi[:, w % WSLOTS, cols], ring_lo[:, w % WSLOTS, cols]), c == 0, c == NC - 1)
                m.then_inc(w_used, 1)

            def q_part(b, j, chunks):
                u, blk, p = b * UNITS + j, j // NC, j % NC
                n = b * NBLK + blk
                if 0 in chunks:
                    wait(pe, q_copied, u - 1)
                    if isinstance(b, int) and b == 0 and j < 2:
                        pe.wait_ge(v_lo_copied, j + 1)
                    if isinstance(b, int) and b == 0 and j == 0:
                        pe.wait_ge(w_lo_made, 3 * NC)
                for c in chunks:
                    if p == 0:
                        pe.wait_ge(act_lo_made, n * NC + c + 1)
                    cols = slice(p * P, (p + 1) * P)
                    m = product(banks[:, j % 2, :], (w_hi[:, c, cols], w_lo[:, c, cols]),
                                (act_hi[:, blk, c, :], act_lo[:, blk, c, :]), c == 0, c == NC - 1)
                if NC - 1 in chunks:
                    m.then_inc(q_done, 1)

            def q_first(b, j):
                q_part(b, j, range(0, NC // 2))

            def q_second(b, j):
                q_part(b, j, range(NC // 2, NC))

            def scores(b, j):
                u, p = b * UNITS + j, j % NC
                pe.wait_ge(q_copied, u + 1)
                wait(pe, masked, u - 1)
                if isinstance(b, int) and b == 0 and j < 2:
                    pe.wait_ge(v_lo_copied, 3 + j)
                if j < NC and p % 2 == 0:
                    pe.wait_ge(k_in[p // 2], 32 * b + 32)
                for t in range(TPB):
                    cols = slice(t * P, (t + 1) * P)
                    m = pe.matmul(banks[:, 2 + j % 2, cols], q_t[:, j % 2, cols], k_diag[:, p, :],
                                  start=True, stop=True)
                m.then_inc(scores_done, 1)

            def transpose_p(b, j):
                u = b * UNITS + j
                pe.wait_ge(probs_done, u + 1)
                wait(pe, p_lo_made, u - 1)
                if isinstance(b, int) and b == 0 and j < 2:
                    pe.wait_ge(v_lo_copied, 5 + j)
                for t in range(TPB):
                    cols = slice(t * P, (t + 1) * P)
                    m = pe.transpose(banks[:, 4 + j % 2, cols], probs[:, j % 4, cols], ident[:])
                m.then_inc(p_transposed, 1)

            def values(b, j):
                u, p = b * UNITS + j, j % NC
                pe.wait_ge(p_lo_made, u + 1)
                wait(pe, o_copied, u - 1)
                if isinstance(b, int) and b == 0 and j < 2:
                    pe.wait_ge(v_lo_copied, 7 + j)
                if j < NC and p % 2 == 0:
                    pe.wait_ge(v_in[p // 2], 64 * b + 64)
                product(banks[:, 6 + j % 2, :], (v_diag_hi[:, p, :], v_diag_lo[:, p, :]),
                        (p_hi[:, j % 2, :], p_lo[:, j % 2, :]), True, True).then_inc(o_done, 1)

            all_batches(pe, [(q_first, 0), (scores, SCORES_LAG), (values, VALUES_LAG), (q_second, 0),
                             (transpose_p, TRANSPOSE_LAG)])

            def out_batch(b):
                for j in range(TILES):
                    v, blk, t = b * TILES + j, j // TPB, j % TPB
                    n = (B + b) * NBLK + blk
                    first = isinstance(b, int) and b == 0 and j == 0
                    wait(pe, out_added, v - 3)
                    if first:
                        pe.wait_ge(o_copied, B * UNITS)
                    for c in range(NC):
                        if t == 0:
                            pe.wait_ge(act_lo_made, n * NC + c + 1)
                        if first:
                            pe.wait_ge(w_lo_made, 3 * NC + c + 1)
                        rows_ = slice(t * P, (t + 1) * P)
                        for h in range(2):
                            cols = slice(h * 512, (h + 1) * 512)
                            m = product(banks[:, 2 * (j % 4) + h, :],
                                        (act_hi[:, blk, c, rows_], act_lo[:, blk, c, rows_]),
                                        (w_hi[:, c, cols], w_lo[:, c, cols]), c == 0, c == NC - 1)
                    m.then_inc(out_done, 1)

            out_batch(0)
            with pe.Fori(1, B - 1) as b:
                out_batch(b)
            out_batch(B - 1)


def kernel(x, ctx_2048, mask_BxS2_bf1, L0_xattn_Wq, L0_xattn_Wk, L0_xattn_Wv, L0_xattn_Wo,
           L0_xattn_ln_gamma, L0_xattn_ln_beta, L0_xattn_gate):
    import numpy as np
    import concourse.bacc as bacc
    from concourse.bass_utils import run_bass_kernel_spmd

    x = np.asarray(x)
    b, t, d = x.shape

    def laid(a):
        return np.ascontiguousarray(a)

    arrays = {
        "x": laid(x.reshape(b * t, d)),
        "x_t": laid(x.transpose(0, 2, 1).reshape(b * d, t)),
        "ctx_x": laid(np.asarray(ctx_2048).reshape(-1, d)),
        "mask": laid(np.asarray(mask_BxS2_bf1)),
        "wq_t": laid(np.asarray(L0_xattn_Wq).T),
        "wk_t": laid(np.asarray(L0_xattn_Wk).T),
        "wv_t": laid(np.asarray(L0_xattn_Wv).T),
        "wo_t": laid(np.asarray(L0_xattn_Wo).T),
        "gamma": laid(np.asarray(L0_xattn_ln_gamma).reshape(-1, P).T),
        "beta": laid(np.asarray(L0_xattn_ln_beta).reshape(-1, P).T),
        "gate": laid(np.asarray(L0_xattn_gate)),
    }
    nc = bacc.Bacc("TRN2", target_bir_lowering=False, num_devices=1)
    args = [nc.dram_tensor(name, a.shape, mybir.dt.from_np(a.dtype), kind="ExternalInput").ap()
            for name, a in arrays.items()]
    out = nc.dram_tensor("out", (b * t, d), F32, kind="ExternalOutput").ap()
    xattn_kernel(nc, *args, out)
    r = run_bass_kernel_spmd(nc, [arrays], core_ids=[0])
    return r.results[0]["out"].reshape(b, t, d)
```

```python
from contextlib import ExitStack

import concourse.bass as bass
from concourse import mybir

ALU = mybir.AluOpType
ACT = mybir.ActivationFunctionType
AX = mybir.AxisListType
F32 = mybir.dt.float32
F32R = mybir.dt.float32r
U8 = mybir.dt.uint8

P = 128
EPS = 1e-5
HEAD = 64


def xattn_kernel(nc, x, x_t, ctx_x, mask, wq_t, wk_t, wv_t, wo_t, gamma, beta, gate, out):
    rows, D = x.shape
    B, S = mask.shape
    T = rows // B
    TB = 512
    NBLK = T // TB
    NC = D // P
    UNITS = NBLK * NC
    TPB = TB // P
    CT = B * S // P
    G = NC // 2
    GROUPS = TPB * 2
    WSLOTS = 4
    SCORES_LAG, TRANSPOSE_LAG, VALUES_LAG, STORE_LAG = 1, 2, 3, 4
    assert NBLK == 2 and NC == 8 and CT == 4 and B * S == TB

    k_scr = nc.dram_tensor("k_scratch", [P, NC, B * S], F32, kind="Internal").ap()
    vhi_scr = nc.dram_tensor("v_hi_scratch", [B * S, D], F32, kind="Internal").ap()
    vlo_scr = nc.dram_tensor("v_lo_scratch", [B * S, D], F32, kind="Internal").ap()
    wsum_scr = nc.dram_tensor("wo_sum_scratch", [5 * D // 2, D // 2], F32, kind="Internal").ap()
    ot_scr = nc.dram_tensor("o_t_scratch", [B * D, T], F32, kind="Internal").ap()

    with ExitStack() as ctx:
        def sb(name, shape, dt=F32):
            return ctx.enter_context(nc.sbuf_tensor(name, shape, dt))

        def sem(name):
            return ctx.enter_context(nc.semaphore(name))

        def sems(name, n):
            return [sem(f"{name}{i}") for i in range(n)]

        banks = ctx.enter_context(nc.psum_tensor("banks", [P, 8, 512], F32))

        w_hi = sb("w_hi", [P, NC, D], F32R)
        w_lo = sb("w_lo", [P, NC, D], F32R)
        act_in = sb("act_in", [P, NC, TB])
        act_hi = sb("act_hi", [P, 2, NC, TB], F32R)
        act_lo = sb("act_lo", [P, 2, NC, TB], F32R)
        w_stage = sb("w_stage", [P, WSLOTS, D])
        k_diag = sb("k_diag", [P, NC, P])
        v_diag_hi = sb("v_diag_hi", [P, NC, P], F32R)
        v_diag_lo = sb("v_diag_lo", [P, NC, P], F32R)
        q_t = sb("q_t", [P, 2, TB])
        probs = sb("probs", [P, 4, TB])
        p_hi = sb("p_hi", [P, 2, TB], F32R)
        p_lo = sb("p_lo", [P, 2, TB], F32R)
        o_t = sb("o_t", [P, 2, TB])
        ident = sb("ident", [P, P])
        mask_u8 = sb("mask_u8", [P, B, S], U8)
        mask_bias = sb("mask_bias", [P, B, S])
        gamma_s = sb("gamma_s", [P, NC])
        beta_s = sb("beta_s", [P, NC])
        gate_s = sb("gate_s", [P, 1])
        tanh_gate = sb("tanh_gate", [P, 1])
        neg_half = sb("neg_half", [P, 1])
        stats = sb("stats", [P, CT, 2, 6])
        mean_var = sb("mean_var", [P, CT, 2])
        var_eps = sb("var_eps", [P, CT])
        rstd = sb("rstd", [P, CT])
        neg_max = sb("neg_max", [P, 2, GROUPS])
        row_sum = sb("row_sum", [P, 2, GROUPS])
        row_rec = sb("row_rec", [P, 2, GROUPS])

        ctx_n = act_in[:].rearrange("p c t -> p (c t)").rearrange("p (i d) -> p i d", i=CT)
        a_hi, a_lo = act_hi[:, 1], act_lo[:, 1]
        ring_hi = act_hi[:, 0].rearrange("p c t -> p (c t)").rearrange("p (s d) -> p s d", s=WSLOTS)
        ring_lo = act_lo[:, 0].rearrange("p c t -> p (c t)").rearrange("p (s d) -> p s d", s=WSLOTS)
        stage_slots = w_stage[:].rearrange("p s (h t) -> p (s h) t", h=2)
        v_out_hi = [stage_slots[:, i, :] for i in range(2 * CT)]
        v_out_lo = [probs[:, i, :] for i in range(4)] + [o_t[:, i, :] for i in range(2)] + \
                   [p_hi[:, i, :].bitcast(F32) for i in range(2)]
        res = [probs[:, 0:2, :], probs[:, 2:4, :], q_t[:, :, :], o_t[:, :, :]]
        block_sum = sb("block_sum", [P, 2, TB])
        neg_tanh_gate = sb("neg_tanh_gate", [P, 1])

        consts_in = sem("consts_in")
        ident_zero = sem("ident_zero")
        ident_made = sem("ident_made")
        diag_zeroed = sem("diag_zeroed")
        mask_step = sem("mask_step")
        gate_ready = sem("gate_ready")
        gate_negated = sem("gate_negated")
        ctx_in = sems("ctx_in", CT)
        stats_made = sem("stats_made")
        mean_made = sem("mean_made")
        var_added = sem("var_added")
        rstd_made = sem("rstd_made")
        normed = sem("normed")
        a_transposed = sem("a_transposed")
        a_scaled = sem("a_scaled")
        a_hi_made = sem("a_hi_made")
        a_lo_made = sem("a_lo_made")
        w_in = sems("w_in", WSLOTS)
        w_hi_made = sem("w_hi_made")
        kv_lo_made = sem("kv_lo_made")
        wq_lo_made = sem("wq_lo_made")
        k_done = sem("k_done")
        wv_used = sem("wv_used")
        k_copied = sem("k_copied")
        k_stored = sems("k_stored", 4)
        v_hi_copied = sem("v_hi_copied")
        v_lo_copied = sem("v_lo_copied")
        v_stored = sems("v_stored", 8)
        k_in = sems("k_in", G)
        v_in = sems("v_in", G)
        act_loaded = sems("act_loaded", NC)
        act_hi_made = sem("act_hi_made")
        act_lo_made = sem("act_lo_made")
        q_done = sem("q_done")
        q_copied = sem("q_copied")
        scores_done = sem("scores_done")
        masked = sem("masked")
        max_done = sem("max_done")
        shifted = sem("shifted")
        exp_done = sem("exp_done")
        sum_done = sem("sum_done")
        rec_done = sem("rec_done")
        probs_done = sem("probs_done")
        p_transposed = sem("p_transposed")
        p_hi_made = sem("p_hi_made")
        p_lo_made = sem("p_lo_made")
        o_done = sem("o_done")
        o_copied = sem("o_copied")
        o_stored = sems("o_stored", 2)
        wo_in = sems("wo_in", NC)
        wo_hi_made = sem("wo_hi_made")
        wo_early_lo = sem("wo_early_lo")
        wo_blocks_in = sems("wo_blocks_in", 2)
        wo_summed = sem("wo_summed")
        wo_sum_stored = sems("wo_sum_stored", 2)
        wo_lo_made = sem("wo_lo_made")
        wo_last_lo_made = sem("wo_last_lo_made")
        o_block_in = sems("o_block_in", 2)
        part_summed = sem("part_summed")
        part_hi_made = sem("part_hi_made")
        part_lo_made = sem("part_lo_made")
        product_done = sem("product_done")
        consumed = sem("consumed")
        res_in = sems("res_in", 4)
        out_stored = sems("out_stored", 4)

        def wait(eng, s, value):
            if not isinstance(value, int) or value > 0:
                eng.wait_ge(s, value)

        def steps(b, lags, count):
            for j in range(count):
                for stage, lag in lags:
                    ju = j - lag
                    if ju >= 0:
                        stage(b, ju)
                    elif not isinstance(b, int) or b > 0:
                        stage(b - 1, ju + count)

        def all_batches(eng, lags, between=lambda j: None, count=UNITS):
            steps(0, lags, count)
            with eng.Fori(1, B - 1) as b:
                steps(b, lags, count)
            steps(B - 1, lags, count)
            for j in range(max(lag for _, lag in lags)):
                for stage, lag in lags:
                    if j < lag:
                        stage(B - 1, j - lag + count)
                between(j)

        def weight_chunk(w):
            c = w % NC
            return (wk_t, wv_t, wq_t)[w // NC][c * P:(c + 1) * P, :]

        def split_target(w):
            if NC <= w < 2 * NC:
                return ring_hi[:, w % WSLOTS, :], ring_lo[:, w % WSLOTS, :]
            return w_hi[:, w % NC, :], w_lo[:, w % NC, :]

        PRODUCTS = {
            1: (((0, 0), +1, (1, 1)), ((0, 0), +1, (1, 1)), (((0, 0), +1), ((1, 1), +1))),
            2: (((1, 0), +1, (1, 1)), ((0, 0), 0, None), (((1, 0), +1), ((1, 1), -1))),
            3: (((0, 0), 0, None), ((0, 1), -1, (1, 1)), (((0, 1), +1), ((1, 1), +1))),
            4: (((1, 1), 0, None), ((1, 0), -1, (0, 0)), (((0, 0), +1), ((1, 0), +1))),
            5: (((0, 0), +1, (0, 1)), ((1, 1), 0, None), (((0, 0), -1), ((0, 1), +1))),
            6: (((1, 0), -1, (0, 0)), ((0, 0), +1, (0, 1)), (((1, 1), +1),)),
            7: (((0, 1), -1, (1, 1)), ((1, 0), +1, (1, 1)), (((0, 0), +1),)),
        }
        ORDER = (2, 5, 3, 7, 4, 1, 6)
        HC = NC // 2
        PAIRS = T // (2 * P)
        ITEMS = len(ORDER) * PAIRS
        RING, PBANKS = 4, 7
        CONSUME_LAG = 4
        EARLY = 2 * HC

        def items(b):
            first = isinstance(b, int) and b == 0
            tiles = [[0, 1], [2], [3]] if first else [[0], [1], [2], [3]]
            return [(m, g) for group in tiles for m in ORDER for g in group]

        def sums_before(b, k):
            return sum(PRODUCTS[m][0][1] != 0 for m, _ in items(b)[:k])

        SUMS = sums_before(0, ITEMS)
        stage_pieces = w_stage[:].rearrange("p s (h t) -> p (s h) t", h=2)
        o_block = [act_in[:], stage_pieces]
        o_sum = block_sum[:].rearrange("p s (c t) -> p s c t", c=HC)

        def o_part(g, rc):
            (r, c), tok = rc, (g % 2) * 2 * P
            return o_block[g // 2][:, c * HC:(c + 1) * HC, tok + r * P:tok + (r + 1) * P]

        def ring(k):
            s = HC + k % RING
            return (act_hi[:, 1, s, :].rearrange("p (c t) -> p c t", c=HC),
                    act_lo[:, 1, s, :].rearrange("p (c t) -> p c t", c=HC))

        def wo_parts(m):
            if m in (2, 5):
                r = slice(0, HC) if m == 2 else slice(HC, NC)
                return act_hi[:, 0, r, :], act_lo[:, 0, r, :]
            if m == 1:
                return act_hi[:, 1, 0:HC, :], act_lo[:, 1, 0:HC, :]
            q = 2 * (3, 7, 4, 6).index(m)
            return (w_hi[:, q:q + 2, :].rearrange("p a (b n) -> p (a b) n", b=2),
                    w_lo[:, q:q + 2, :].rearrange("p a (b n) -> p (a b) n", b=2))

        SUMMED = ORDER[2:]
        SUM_PIECES = len(SUMMED) * HC

        def sum_pieces(b, j):
            if not (isinstance(b, int) and b == 0):
                return []
            return [(n, n // len(SUMMED), n % len(SUMMED)) for n in (2 * j - 8, 2 * j - 7)
                    if 0 <= n < SUM_PIECES]

        def block_piece(c, rc):
            return stage_pieces[:, (c % 2) * HC + 2 * rc[0] + rc[1], :]

        def wsum_rows(i, c):
            return wsum_scr[(i * HC + c) * P:(i * HC + c + 1) * P, :]

        def wo_split_at(b, k):
            return [k // 2] if isinstance(b, int) and b == 0 and k % 2 == 1 and 0 < k // 2 < len(SUMMED) else []

        def pool_wo_split_at(b, k):
            late = {3: [1], 7: [2, 3], 9: [4]}
            return late.get(k, []) if isinstance(b, int) and b == 0 else []

        STARTED = 4

        def wo_lo_count(i, c):
            return (wo_lo_made, i * (HC - 1) + c + 1) if c < HC - 1 else (wo_last_lo_made, i + 1)

        def is_last_unit(b, j):
            return isinstance(b, int) and b == B - 1 and j == UNITS - 1

        block = ctx.enter_context(nc.Block())

        @block.sync
        def _(sp):
            def load_weight(w):
                if w - WSLOTS >= 2 * NC:
                    sp.wait_ge(wq_lo_made, w - WSLOTS - 2 * NC + 1)
                else:
                    wait(sp, kv_lo_made, w - WSLOTS + 1)
                sp.dma_start(w_stage[:, w % WSLOTS, :], weight_chunk(w)).then_inc(w_in[w % WSLOTS], 16)

            def load_act(b, blk, c, src):
                sp.dma_start(act_in[:, c, :], src[bass.ds(b * D + c * P, P), blk * TB:(blk + 1) * TB]
                             ).then_inc(act_loaded[c], 16)

            def load_k(b, q):
                for h in range(2):
                    r = slice(h * HEAD, (h + 1) * HEAD)
                    sp.dma_start(k_diag[r, 2 * q:2 * q + 2, r],
                                 k_scr[r, 2 * q:2 * q + 2, bass.ds(b * S, S)]).then_inc(k_in[q], 16)

            def load_v(b, q):
                for h in range(2):
                    r = slice(h * HEAD, (h + 1) * HEAD)
                    for diag, scr in ((v_diag_hi, vhi_scr), (v_diag_lo, vlo_scr)):
                        src = scr[bass.ds(b * S, S), 2 * q * P:(2 * q + 2) * P].rearrange(
                            "s (g e) -> s g e", g=2)[:, :, r]
                        sp.dma_start(diag[r, 2 * q:2 * q + 2, r].bitcast(F32), src).then_inc(v_in[q], 16)

            for i in range(CT):
                sp.dma_start(ctx_n[:, i, :], ctx_x[i * P:(i + 1) * P, :]).then_inc(ctx_in[i], 16)
            sp.dma_start(gamma_s[:], gamma).then_inc(consts_in, 16)
            sp.dma_start(beta_s[:], beta).then_inc(consts_in, 16)
            sp.dma_start(gate_s[:], gate.partition_broadcast(P)).then_inc(consts_in, 16)
            sp.dma_start(mask_u8[:], mask.partition_broadcast(P)).then_inc(consts_in, 16)
            for w in range(13):
                load_weight(w)
            for p in range(NC):
                sp.wait_ge(k_copied, p + 1)
                sp.dma_start(k_scr[:, p, :], probs[:, p % 4, :]).then_inc(k_stored[p % 4], 16)
            sp.wait_ge(a_transposed, NC)
            for c in range(NC):
                load_act(0, 0, c, x_t)
            for w in range(13, 24):
                load_weight(w)
            for s in k_stored:
                sp.wait_ge(s, 32)
            sp.wait_ge(diag_zeroed, 3)
            for q in range(G):
                load_k(0, q)
            def load_second_block(chunks):
                for c in chunks:
                    sp.wait_ge(act_lo_made, c + 1)
                    load_act(0, 1, c, x_t)

            load_second_block(range(0, NC // 2))
            for i in range(2 * CT):
                sp.wait_ge(v_lo_copied, i + 1)
                r, cols = slice(i // 2 * P, (i // 2 + 1) * P), slice(i % 2 * 512, (i % 2 + 1) * 512)
                sp.dma_start(vhi_scr[r, cols], v_out_hi[i]).then_inc(v_stored[i], 16)
                sp.dma_start(vlo_scr[r, cols], v_out_lo[i]).then_inc(v_stored[i], 16)
            load_second_block(range(NC // 2, NC))
            for s in v_stored:
                sp.wait_ge(s, 32)
            for q in range(G):
                load_v(0, q)

            def load_block_pieces(c):
                for r in range(2):
                    for col in range(2):
                        sp.dma_start(block_piece(c, (r, col)),
                                     wo_t[(r * HC + c) * P:(r * HC + c + 1) * P, col * 512:(col + 1) * 512]
                                     ).then_inc(wo_blocks_in[c % 2], 16)

            load_block_pieces(0)
            load_block_pieces(1)

            def store_sum_pieces(b, j):
                for n, c, i in sum_pieces(b, j):
                    sp.wait_ge(wo_summed, n + 1)
                    sp.dma_start(wsum_rows(i, c), block_sum[:, n % 2, :]).then_inc(wo_sum_stored[n % 2], 16)
                    if i == len(SUMMED) - 1 and c + 2 < HC:
                        load_block_pieces(c + 2)
                    if n == SUM_PIECES - 1:
                        for half in range(2):
                            for c_ in range(HC):
                                sp.dma_start(stage_pieces[:, half * HC + c_, :],
                                             wo_t[(half * HC + c_) * P:(half * HC + c_ + 1) * P,
                                                  half * 512:(half + 1) * 512]).then_inc(wo_in[half * HC + c_], 16)

            def load_wo_sum(i):
                for c in range(HC):
                    if i < 2:
                        sp.wait_ge(wo_early_lo, i * HC + c + 1)
                    else:
                        sp.wait_ge(*wo_lo_count(i - 2, c))
                    sp.dma_start(stage_pieces[:, i % 2 * HC + c, :], wsum_rows(i, c)
                                 ).then_inc(wo_in[i % 2 * HC + c], 16)

            def load_first_sum(b, j):
                if isinstance(b, int) and b == B - 1 and j == NC + HC + 1:
                    for s in wo_sum_stored:
                        sp.wait_ge(s, 16 * SUM_PIECES // 2)
                    load_wo_sum(0)

            def store_o(b, j):
                u = b * UNITS + j
                sp.wait_ge(o_copied, u + 1)
                sp.dma_start(ot_scr[bass.ds(b * D + j % NC * P, P), j // NC * TB:(j // NC + 1) * TB],
                             o_t[:, j % 2, :]).then_inc(o_stored[j % 2], 16)

            def load_next_kv(b, j):
                if j < NC or j % 2 == 0 or (isinstance(b, int) and b == B - 1):
                    return
                sp.wait_ge(o_done, b * UNITS + j + 1)
                load_k(b + 1, (j - NC) // 2)
                load_v(b + 1, (j - NC) // 2)

            def load_block_after_next(b, j):
                blk, c = j // NC, j % NC
                if isinstance(b, int) and b == B - 1 and blk == 1:
                    return
                sp.wait_ge(act_lo_made, (b * NBLK + blk + 1) * NC + c + 1)
                if isinstance(b, int) and b == B - 1:
                    sp.wait_ge(o_stored[c % 2], 16 * ((blk * NC + c) // 2 + 1))
                    load_act(0, blk, c, ot_scr)
                else:
                    load_act(b + 1, blk, c, x_t)

            def tile_rows(ap, b, g, r):
                return ap[bass.ds((b * 2 * PAIRS + 2 * g + r) * P, P), :].rearrange("p (a n) -> p a n", a=2)

            def load_res(b, g):
                for r in range(2):
                    t = 2 * (g % 2) + r
                    src = tile_rows(x, b, g, r)
                    wait(sp, out_stored[t], 16 * (2 * b + g // 2))
                    sp.dma_start(res[t], src).then_inc(res_in[t], 16)

            def after_unit(j):
                if j == 0:
                    load_wo_sum(1)
                if j == 1:
                    sp.wait_ge(p_transposed, B * UNITS)
                    load_res(0, 0)
                if j == 3:
                    load_wo_sum(2)

            all_batches(sp, [(load_block_after_next, 0), (store_sum_pieces, 0), (load_first_sum, 0),
                             (store_o, STORE_LAG), (load_next_kv, STORE_LAG)], after_unit)

            for s in o_stored:
                sp.wait_ge(s, 16 * B * UNITS // 2)

            def store_out(b, g):
                first = isinstance(b, int) and b == 0 and g < 2
                to = [tile_rows(out, b, g, r) for r in range(2)]
                sp.wait_ge(consumed, 2 * len(ORDER) if first else b * ITEMS + (g + 1) * len(ORDER))
                for r in range(2):
                    t = 2 * (g % 2) + r
                    sp.dma_start(to[r], res[t]).then_inc(out_stored[t], 16)

            def store_last_out():
                g, t = PAIRS - 1, 2 * ((PAIRS - 1) % 2)
                low, high = (tile_rows(out, B - 1, g, r) for r in range(2))
                done = B * ITEMS - len(ORDER) + 1
                sp.wait_ge(consumed, done + ORDER.index(4))
                sp.dma_start(high[:, 0, :], res[t + 1][:, 0, :]).then_inc(out_stored[t + 1], 16)
                sp.wait_ge(consumed, done + ORDER.index(1))
                sp.dma_start(low, res[t]).then_inc(out_stored[t], 16)
                sp.wait_ge(consumed, done + ORDER.index(6))
                sp.dma_start(high[:, 1, :], res[t + 1][:, 1, :]).then_inc(out_stored[t + 1], 16)

            def o_rows(b, blk):
                return ot_scr[bass.ds(b * D, D), blk * TB:(blk + 1) * TB].rearrange("(c p) t -> p c t", p=P)

            def out_batch(b):
                src = o_rows(b, 1)
                if isinstance(b, int) and b == 0:
                    sp.wait_ge(*wo_lo_count(len(SUMMED) - 1, HC - 2))
                    sp.wait_ge(*wo_lo_count(len(SUMMED) - 1, HC - 1))
                else:
                    sp.wait_ge(part_lo_made, b * ITEMS)
                sp.dma_start(o_block[1], src).then_inc(o_block_in[1], 16)
                for g in range(2):
                    store_out(b, g)
                    load_res(b, g + 2)
                if not (isinstance(b, int) and b == B - 1):
                    src = o_rows(b + 1, 0)
                    sp.wait_ge(part_lo_made, b * ITEMS + ITEMS // 2)
                    sp.dma_start(o_block[0], src).then_inc(o_block_in[0], 16)
                for g in range(2, PAIRS):
                    if isinstance(b, int) and b == B - 1 and g == PAIRS - 1:
                        store_last_out()
                    else:
                        store_out(b, g)
                    if not (isinstance(b, int) and b == B - 1):
                        load_res(b + 1, g - 2)

            load_res(0, 1)
            load_wo_sum(3)
            load_wo_sum(4)
            out_batch(0)
            with sp.Fori(1, B - 1) as b:
                out_batch(b)
            out_batch(B - 1)
            for t, s in enumerate(out_stored):
                sp.wait_ge(s, 16 * (B * PAIRS // 2 + (t == 3)))

        @block.gpsimd
        def _(pool):
            nc.gpsimd.memset(ident[:], 0.0).then_inc(ident_zero, 1)
            pool.wait_ge(ident_zero, 1)
            nc.gpsimd.affine_select(out=ident[:], in_=ident[:], compare_op=ALU.not_equal, fill=1.0, base=0,
                                    pattern=[[-1, P]], channel_multiplier=1).then_inc(ident_made, 1)
            nc.gpsimd.memset(neg_half[:], -0.5).then_inc(ident_zero, 1)
            pool.wait_ge(ident_zero, 2)
            for i in range(CT):
                pool.wait_ge(var_added, i + 1)
                nc.gpsimd.tensor_tensor(rstd[:, i:i + 1], var_eps[:, i:i + 1], neg_half[:], ALU.pow
                                        ).then_inc(rstd_made, 1)

            for w in range(2 * NC):
                if w == NC:
                    nc.gpsimd.memset(k_diag[:], 0.0).then_inc(diag_zeroed, 1)
                    nc.gpsimd.memset(v_diag_hi[:].bitcast(F32), 0.0).then_inc(diag_zeroed, 1)
                    nc.gpsimd.memset(v_diag_lo[:].bitcast(F32), 0.0).then_inc(diag_zeroed, 1)
                hi, lo = split_target(w)
                pool.wait_ge(w_hi_made, w + 1)
                nc.gpsimd.tensor_tensor(lo, w_stage[:, w % WSLOTS, :], hi.bitcast(F32), ALU.subtract
                                        ).then_inc(kv_lo_made, 1)

            def split_lo(n, par, c):
                pool.wait_ge(act_hi_made, n * NC + c + 1)
                nc.gpsimd.tensor_tensor(act_lo[:, par, c, :], act_in[:, c, :], act_hi[:, par, c, :].bitcast(F32),
                                        ALU.subtract).then_inc(act_lo_made, 1)

            for c in range(NC):
                split_lo(0, 0, c)

            def normalise(b, j):
                u = b * UNITS + j
                pr = probs[:, j % 4, :].rearrange("p (g s) -> p g s", s=S)
                rec = row_rec[:, j % 2, :].unsqueeze(2).to_broadcast([P, GROUPS, S])
                pool.wait_ge(rec_done, u + 1)
                nc.gpsimd.tensor_tensor(pr, pr, rec, ALU.mult).then_inc(probs_done, 1)

            def split_next(b, j):
                if isinstance(b, int) and b == B - 1 and j >= NC:
                    k = j - NC
                    hi, lo = wo_parts(ORDER[k // HC])
                    pool.wait_ge(wo_hi_made, k + 1)
                    nc.gpsimd.tensor_tensor(lo[:, k % HC, :], stage_pieces[:, k, :], hi[:, k % HC, :].bitcast(F32),
                                            ALU.subtract).then_inc(wo_early_lo, 1)
                    return
                split_lo(b * NBLK + j // NC + 1, (j // NC + 1) % 2, j % NC)

            def sum_o(b, k):
                m, g = items(b)[k]
                (one, sign, other), _, _ = PRODUCTS[m]
                if sign == 0:
                    return
                n = sums_before(b, k)
                if n >= 2 or not isinstance(b, int) or b > 0:
                    bb, nn = (b, n - 2) if n >= 2 else (b - 1, n - 2 + SUMS)
                    kk = max(i for i in range(ITEMS) if sums_before(bb, i) == nn
                             and PRODUCTS[items(bb)[i][0]][0][1] != 0)
                    pool.wait_ge(part_lo_made, bb * ITEMS + kk + 1)
                if isinstance(b, int) and b == 0 and g < 2:
                    if k == 0:
                        for c in range(NC):
                            pool.wait_ge(act_loaded[c], 16 * (B * NBLK + 1))
                        for s in wo_sum_stored:
                            pool.wait_ge(s, 16 * SUM_PIECES // 2)
                elif k % len(ORDER) == 0:
                    pool.wait_ge(o_block_in[g // 2], 16 * (b + (1 if g // 2 else 0)))
                nc.gpsimd.tensor_tensor(o_sum[:, n % 2], o_part(g, one), o_part(g, other),
                                        ALU.add if sign > 0 else ALU.subtract).then_inc(part_summed, 1)

            def sum_wo(b, j):
                for n, c, i in sum_pieces(b, j):
                    if i == 0:
                        pool.wait_ge(wo_blocks_in[c % 2], 64 * (c // 2 + 1))
                    wait(pool, wo_sum_stored[n % 2], 16 * (n // 2))
                    one, sign, other = PRODUCTS[SUMMED[i]][1]
                    nc.gpsimd.tensor_tensor(block_sum[:, n % 2, :], block_piece(c, one), block_piece(c, other),
                                            ALU.add if sign > 0 else ALU.subtract).then_inc(wo_summed, 1)

            def split_wo_lo(i):
                hi, lo = wo_parts(SUMMED[i])
                for c in range(HC - 1):
                    pool.wait_ge(wo_hi_made, EARLY + i * HC + c + 1)
                    nc.gpsimd.tensor_tensor(lo[:, c, :], stage_pieces[:, i % 2 * HC + c, :],
                                            hi[:, c, :].bitcast(F32), ALU.subtract).then_inc(wo_lo_made, 1)

            def first_sums_o(b, j):
                if is_last_unit(b, j):
                    sum_o(0, 0)
                    sum_o(0, 1)

            def next_item(b, k):
                if not (isinstance(b, int) and b == 0 and k < STARTED):
                    sum_o(b, k)
                for i in pool_wo_split_at(b, k):
                    split_wo_lo(i)

            all_batches(pool, [(split_next, 0), (first_sums_o, 1), (normalise, TRANSPOSE_LAG), (sum_wo, 0)],
                        lambda j: sum_o(0, j + 2))
            split_wo_lo(0)
            all_batches(pool, [(next_item, 0)], count=ITEMS)

        @block.scalar
        def _(act):
            def split_weight_hi(w):
                act.wait_ge(w_in[w % WSLOTS], 16 * (w // WSLOTS + 1))
                if NC + WSLOTS <= w < 2 * NC:
                    act.wait_ge(wv_used, w - NC - WSLOTS + 1)
                elif w == 2 * NC:
                    act.wait_ge(k_done, 2)
                nc.scalar.copy(split_target(w)[0], w_stage[:, w % WSLOTS, :]).then_inc(w_hi_made, 1)

            def split_hi(n, par, c):
                nc.scalar.copy(act_hi[:, par, c, :], act_in[:, c, :]).then_inc(act_hi_made, 1)

            for w in range(WSLOTS):
                split_weight_hi(w)
            act.wait_ge(consts_in, 64)
            nc.scalar.activation(tanh_gate[:], gate_s[:], ACT.Tanh).then_inc(gate_ready, 1)
            for c in range(NC):
                act.wait_ge(a_scaled, c + 1)
                nc.scalar.copy(a_hi[:, c, :], q_t[:, c % 2, :]).then_inc(a_hi_made, 1)
                if c < NC - WSLOTS:
                    split_weight_hi(WSLOTS + c)

            def copy_k(half):
                act.wait_ge(k_done, half + 1)
                for p in range(4 * half, 4 * half + 4):
                    if p >= 4:
                        act.wait_ge(k_stored[p % 4], 16)
                    nc.scalar.mul(probs[:, p % 4, :], banks[:, p, :], HEAD ** -0.5).then_inc(k_copied, 1)

            copy_k(0)
            for w in range(NC, NC + WSLOTS):
                split_weight_hi(w)
            copy_k(1)
            for w in range(NC + WSLOTS, 3 * NC):
                split_weight_hi(w)
            def split_first_block(chunks):
                for c in chunks:
                    act.wait_ge(act_loaded[c], 16)
                    act.wait_ge(wv_used, 5 + c // 2)
                    split_hi(0, 0, c)

            def copy_v_hi(banks_):
                for i in banks_:
                    nc.scalar.copy(v_out_hi[i].bitcast(F32R), banks[:, i, :]).then_inc(v_hi_copied, 1)

            split_first_block(range(0, NC - 2))
            act.wait_ge(wv_used, NC)
            act.wait_ge(wq_lo_made, NC)
            copy_v_hi(range(0, 1))
            split_first_block(range(NC - 2, NC))
            copy_v_hi(range(1, 2 * CT))

            def copy_q(b, j):
                u = b * UNITS + j
                act.wait_ge(q_done, u + 1)
                wait(act, scores_done, u - 1)
                nc.scalar.copy(q_t[:, j % 2, :], banks[:, j % 2, :]).then_inc(q_copied, 1)

            def split_next(b, j):
                n = b * NBLK + j // NC
                if isinstance(b, int) and b == B - 1 and j >= NC:
                    k = j - NC
                    act.wait_ge(wo_in[k], 16)
                    if k == 0:
                        act.wait_ge(q_done, n * NC)
                    nc.scalar.copy(wo_parts(ORDER[k // HC])[0][:, k % HC, :], stage_pieces[:, k, :]
                                   ).then_inc(wo_hi_made, 1)
                    return
                act.wait_ge(act_loaded[j % NC], 16 * (n + 2))
                if j % NC == 0:
                    if isinstance(b, int) and b == 0 and j == 0:
                        act.wait_ge(wv_used, NC)
                    else:
                        act.wait_ge(q_done, n * NC)
                split_hi(n + 1, (j // NC + 1) % 2, j % NC)

            def exponential(b, j):
                u = b * UNITS + j
                act.wait_ge(shifted, u + 1)
                nc.scalar.activation(probs[:, j % 4, :], probs[:, j % 4, :], ACT.Exp).then_inc(exp_done, 1)

            def split_p_hi(b, j):
                u = b * UNITS + j
                act.wait_ge(p_transposed, u + 1)
                wait(act, o_done, u - 1)
                if isinstance(b, int) and b == 0 and j < 2:
                    act.wait_ge(v_stored[6 + j], 32)
                nc.scalar.copy(p_hi[:, j % 2, :], banks[:, 4 + j % 2, :]).then_inc(p_hi_made, 1)

            def copy_o(b, j):
                u = b * UNITS + j
                act.wait_ge(o_done, u + 1)
                wait(act, o_stored[j % 2], b * (16 * UNITS // 2) + 16 * (j // 2))
                if isinstance(b, int) and b == 0 and j < 2:
                    act.wait_ge(v_stored[4 + j], 32)
                nc.scalar.copy(o_t[:, j % 2, :], banks[:, 6 + j % 2, :]).then_inc(o_copied, 1)

            def split_o_hi(b, k):
                m, g = items(b)[k]
                (one, sign, _), _, _ = PRODUCTS[m]
                if isinstance(b, int) and b == 0 and k < RING:
                    act.wait_ge(q_done, B * UNITS)
                else:
                    act.wait_ge(product_done, b * ITEMS + k - RING + 1)
                n = sums_before(b, k)
                if sign:
                    act.wait_ge(part_summed, b * SUMS + n + 1)
                    src = o_sum[:, n % 2]
                else:
                    act.wait_ge(part_summed, b * SUMS + n)
                    src = o_part(g, one)
                nc.scalar.copy(ring(k)[0], src).then_inc(part_hi_made, 1)

            def split_wo_hi(i):
                for c in range(HC):
                    piece = i % 2 * HC + c
                    act.wait_ge(wo_in[piece], 16 * (i // 2 + 2))
                    nc.scalar.copy(wo_parts(SUMMED[i])[0][:, c, :], stage_pieces[:, piece, :]).then_inc(wo_hi_made, 1)

            def first_o_hi(b, j):
                if is_last_unit(b, j):
                    split_o_hi(0, 0)

            def after_unit(j):
                if j + 1 < STARTED:
                    split_o_hi(0, j + 1)
                if j == 2:
                    split_wo_hi(0)

            def next_item(b, k):
                if not (isinstance(b, int) and b == 0 and k < STARTED):
                    split_o_hi(b, k)
                for i in wo_split_at(b, k):
                    split_wo_hi(i)

            all_batches(act, [(copy_q, 1), (split_p_hi, VALUES_LAG), (first_o_hi, 1), (split_next, 0),
                              (copy_o, STORE_LAG), (exponential, SCORES_LAG)],
                        after_unit)
            all_batches(act, [(next_item, 0)], count=ITEMS)

        @block.vector
        def _(dve):
            def normalise_context(i):
                dve.wait_ge(rstd_made, i + 1)
                nc.vector.tensor_scalar(ctx_n[:, i, :], ctx_n[:, i, :], mean_var[:, i, 0:1], rstd[:, i:i + 1],
                                        ALU.subtract, ALU.mult).then_inc(normed, 1)

            for i in range(CT):
                dve.wait_ge(ctx_in[i], 16)
                for h in range(2):
                    nc.vector.bn_stats(stats[:, i, h, :], ctx_n[:, i, h * 512:(h + 1) * 512]).then_inc(stats_made, 1)
                dve.wait_ge(stats_made, 2 * i + 2)
                nc.vector.bn_aggr(mean_var[:, i, :], stats[:, i, :, :]).then_inc(mean_made, 1)
                dve.wait_ge(mean_made, i + 1)
                nc.vector.tensor_scalar(var_eps[:, i:i + 1], mean_var[:, i, 1:2], EPS, None, ALU.add
                                        ).then_inc(var_added, 1)
                if i > 0:
                    normalise_context(i - 1)
            normalise_context(CT - 1)

            def split_weight_lo(w):
                hi, lo = split_target(w)
                dve.wait_ge(w_hi_made, w + 1)
                nc.vector.tensor_tensor(lo, w_stage[:, w % WSLOTS, :], hi.bitcast(F32), ALU.subtract
                                        ).then_inc(wq_lo_made, 1)

            dve.wait_ge(consts_in, 64)
            for c in range(NC):
                dve.wait_ge(a_transposed, c + 1)
                if c >= 2:
                    dve.wait_ge(a_lo_made, c - 1)
                nc.vector.tensor_scalar(q_t[:, c % 2, :], banks[:, 4 + c % 4, :], gamma_s[:, c:c + 1], beta_s[:, c:c + 1],
                                        ALU.mult, ALU.add).then_inc(a_scaled, 1)
                dve.wait_ge(a_hi_made, c + 1)
                nc.vector.tensor_tensor(a_lo[:, c, :], q_t[:, c % 2, :], a_hi[:, c, :].bitcast(F32), ALU.subtract
                                        ).then_inc(a_lo_made, 1)
            bias_flat, mask_flat = mask_bias[:], mask_u8[:]
            nc.vector.tensor_scalar(bias_flat, mask_flat, -1.0, 3e38, ALU.add, ALU.mult).then_inc(mask_step, 1)
            dve.wait_ge(mask_step, 1)
            nc.vector.tensor_scalar(bias_flat, bias_flat, 3e38, None, ALU.mult).then_inc(mask_step, 1)

            for w in range(2 * NC, 3 * NC):
                split_weight_lo(w)
            for s in k_stored:
                dve.wait_ge(s, 32)
            for i in range(2 * CT):
                dve.wait_ge(v_hi_copied, i + 1)
                nc.vector.tensor_tensor(v_out_lo[i].bitcast(F32R), banks[:, i, :], v_out_hi[i],
                                        ALU.subtract).then_inc(v_lo_copied, 1)

            def split_p_lo(b, j):
                u = b * UNITS + j
                dve.wait_ge(p_hi_made, u + 1)
                nc.vector.tensor_tensor(p_lo[:, j % 2, :], banks[:, 4 + j % 2, :], p_hi[:, j % 2, :].bitcast(F32),
                                        ALU.subtract).then_inc(p_lo_made, 1)

            def grouped(j):
                return probs[:, j % 4, :].rearrange("p (g s) -> p g s", s=S)

            def sum_rows(b, j):
                u = b * UNITS + j
                dve.wait_ge(exp_done, u + 1)
                nc.vector.reduce_sum(row_sum[:, j % 2, :], grouped(j), AX.X).then_inc(sum_done, 1)

            def invert_sums(b, j):
                u = b * UNITS + j
                dve.wait_ge(sum_done, u + 1)
                wait(dve, probs_done, u - 1)
                nc.vector.reciprocal(row_rec[:, j % 2, :], row_sum[:, j % 2, :]).then_inc(rec_done, 1)

            def mask_scores(b, j):
                u = b * UNITS + j
                dve.wait_ge(scores_done, u + 1)
                wait(dve, p_transposed, u - 3)
                if isinstance(b, int) and b == 0 and j < 4:
                    dve.wait_ge(v_stored[j], 32)
                bias = mask_bias[:, bass.ds(b, 1), :].to_broadcast([P, GROUPS, S])
                scores = banks[:, 2 + j % 2, :].rearrange("p (g s) -> p g s", s=S)
                nc.vector.tensor_tensor(grouped(j), scores, bias, ALU.add).then_inc(masked, 1)

            def row_max(b, j):
                u = b * UNITS + j
                dve.wait_ge(masked, u + 1)
                nc.vector.tensor_reduce(neg_max[:, j % 2, :], grouped(j), AX.X, ALU.max, negate=True
                                        ).then_inc(max_done, 1)

            def shift(b, j):
                u = b * UNITS + j
                dve.wait_ge(max_done, u + 1)
                top = neg_max[:, j % 2, :].unsqueeze(2).to_broadcast([P, GROUPS, S])
                nc.vector.tensor_tensor(grouped(j), grouped(j), top, ALU.add).then_inc(shifted, 1)

            def split_o_lo(b, k):
                m, g = items(b)[k]
                (one, sign, _), _, _ = PRODUCTS[m]
                hi, lo = ring(k)
                dve.wait_ge(part_hi_made, b * ITEMS + k + 1)
                src = o_sum[:, sums_before(b, k) % 2] if sign else o_part(g, one)
                nc.vector.tensor_tensor(lo, src, hi.bitcast(F32), ALU.subtract).then_inc(part_lo_made, 1)

            def first_o_lo(b, j):
                if is_last_unit(b, j):
                    split_o_lo(0, 0)

            all_batches(dve, [(sum_rows, TRANSPOSE_LAG), (split_p_lo, VALUES_LAG), (invert_sums, TRANSPOSE_LAG),
                              (first_o_lo, 1), (mask_scores, SCORES_LAG), (row_max, SCORES_LAG), (shift, SCORES_LAG)],
                        lambda j: split_o_lo(0, j + 1))
            dve.wait_ge(gate_ready, 1)
            nc.vector.tensor_scalar(neg_tanh_gate[:], tanh_gate[:], -1.0, None, ALU.mult).then_inc(gate_negated, 1)
            dve.wait_ge(gate_negated, 1)

            def split_last_wo_lo(i):
                (hi, lo), c = wo_parts(SUMMED[i]), HC - 1
                dve.wait_ge(wo_hi_made, EARLY + (i + 1) * HC)
                nc.vector.tensor_tensor(lo[:, c, :], stage_pieces[:, i % 2 * HC + c, :], hi[:, c, :].bitcast(F32),
                                        ALU.subtract).then_inc(wo_last_lo_made, 1)

            def consume(b, k):
                m, g = items(b)[k]
                dve.wait_ge(product_done, b * ITEMS + k + 1)
                wait(dve, consumed, b * ITEMS + k)
                if m == ORDER[0]:
                    for r in range(2):
                        dve.wait_ge(res_in[2 * (g % 2) + r], 16 * (2 * b + g // 2 + 1))
                uses = PRODUCTS[m][2]
                for (r, c), sign in uses:
                    to = res[2 * (g % 2) + r][:, c, :]
                    by = tanh_gate if sign > 0 else neg_tanh_gate
                    last = nc.vector.scalar_tensor_tensor(out=to, in0=banks[:, k % PBANKS, :], scalar=by[:, 0:1],
                                                          in1=to, op0=ALU.mult, op1=ALU.add)
                last.then_inc(consumed, 1)

            def next_item(b, k):
                if not (isinstance(b, int) and b == 0 and k < STARTED):
                    split_o_lo(b, k)
                for i in wo_split_at(b, k):
                    split_last_wo_lo(i)

            split_last_wo_lo(0)
            all_batches(dve, [(next_item, 0), (consume, CONSUME_LAG)], count=ITEMS)

        @block.tensor
        def _(pe):
            def product(to, w_parts, m_parts, first, last):
                (wh, wl), (mh, ml) = w_parts, m_parts
                pe.matmul(to, wl, mh, start=first, stop=False)
                pe.matmul(to, wh, ml, start=False, stop=False)
                return pe.matmul(to, wh, mh, start=False, stop=last)

            pe.wait_ge(ident_made, 1)
            def transpose_context(c):
                if c >= 4:
                    pe.wait_ge(a_scaled, c - 3)
                for i in range(CT):
                    if c == 0:
                        pe.wait_ge(normed, i + 1)
                    t = pe.transpose(banks[:, 4 + c % 4, i * P:(i + 1) * P], ctx_n[:, i, c * P:(c + 1) * P], ident[:])
                t.then_inc(a_transposed, 1)

            def k_chunk(half, c):
                if half == 0:
                    pe.wait_ge(kv_lo_made, c + 1)
                    pe.wait_ge(a_lo_made, c + 1)
                for p in range(4 * half, 4 * half + 4):
                    cols = slice(p * P, (p + 1) * P)
                    m = product(banks[:, p, :], (w_hi[:, c, cols], w_lo[:, c, cols]),
                                (a_hi[:, c, :], a_lo[:, c, :]), c == 0, c == NC - 1)
                if c == NC - 1:
                    m.then_inc(k_done, 1)

            for c in range(4):
                transpose_context(c)
            for c in range(NC):
                k_chunk(0, c)
                if c < 4:
                    transpose_context(4 + c)
            for c in range(NC):
                k_chunk(1, c)
            for c in range(NC):
                w = NC + c
                pe.wait_ge(kv_lo_made, w + 1)
                for i in range(2 * CT):
                    if c == 0:
                        pe.wait_ge(k_copied, i + 1)
                    rows_, cols = slice(i // 2 * P, (i // 2 + 1) * P), slice(i % 2 * 512, (i % 2 + 1) * 512)
                    m = product(banks[:, i, :], (a_hi[:, c, rows_], a_lo[:, c, rows_]),
                                (ring_hi[:, w % WSLOTS, cols], ring_lo[:, w % WSLOTS, cols]), c == 0, c == NC - 1)
                m.then_inc(wv_used, 1)

            def q_part(b, j, chunks):
                u, blk, p = b * UNITS + j, j // NC, j % NC
                n = b * NBLK + blk
                if 0 in chunks:
                    wait(pe, q_copied, u - 1)
                    if isinstance(b, int) and b == 0 and j < 2:
                        pe.wait_ge(v_lo_copied, j + 1)
                    if isinstance(b, int) and b == 0 and j == 0:
                        pe.wait_ge(wq_lo_made, NC)
                for c in chunks:
                    if p == 0:
                        pe.wait_ge(act_lo_made, n * NC + c + 1)
                    cols = slice(p * P, (p + 1) * P)
                    m = product(banks[:, j % 2, :], (w_hi[:, c, cols], w_lo[:, c, cols]),
                                (act_hi[:, blk, c, :], act_lo[:, blk, c, :]), c == 0, c == NC - 1)
                if NC - 1 in chunks:
                    m.then_inc(q_done, 1)

            def q_first(b, j):
                q_part(b, j, range(0, NC // 2))

            def q_second(b, j):
                q_part(b, j, range(NC // 2, NC))

            def scores(b, j):
                u, p = b * UNITS + j, j % NC
                pe.wait_ge(q_copied, u + 1)
                wait(pe, masked, u - 1)
                if isinstance(b, int) and b == 0 and j < 2:
                    pe.wait_ge(v_lo_copied, 3 + j)
                if j < NC and p % 2 == 0:
                    pe.wait_ge(k_in[p // 2], 32 * b + 32)
                for t in range(TPB):
                    cols = slice(t * P, (t + 1) * P)
                    m = pe.matmul(banks[:, 2 + j % 2, cols], q_t[:, j % 2, cols], k_diag[:, p, :],
                                  start=True, stop=True)
                m.then_inc(scores_done, 1)

            def transpose_p(b, j):
                u = b * UNITS + j
                pe.wait_ge(probs_done, u + 1)
                wait(pe, p_lo_made, u - 1)
                if isinstance(b, int) and b == 0 and j < 2:
                    pe.wait_ge(v_lo_copied, 5 + j)
                for t in range(TPB):
                    cols = slice(t * P, (t + 1) * P)
                    m = pe.transpose(banks[:, 4 + j % 2, cols], probs[:, j % 4, cols], ident[:])
                m.then_inc(p_transposed, 1)

            def values(b, j):
                u, p = b * UNITS + j, j % NC
                pe.wait_ge(p_lo_made, u + 1)
                wait(pe, o_copied, u - 1)
                if isinstance(b, int) and b == 0 and j < 2:
                    pe.wait_ge(v_lo_copied, 7 + j)
                if j < NC and p % 2 == 0:
                    pe.wait_ge(v_in[p // 2], 64 * b + 64)
                product(banks[:, 6 + j % 2, :], (v_diag_hi[:, p, :], v_diag_lo[:, p, :]),
                        (p_hi[:, j % 2, :], p_lo[:, j % 2, :]), True, True).then_inc(o_done, 1)

            def out_product(b, k):
                m, g = items(b)[k]
                first = isinstance(b, int) and b == 0
                if first and k < PBANKS:
                    pe.wait_ge((q_copied, q_copied, masked, masked, p_lo_made, p_lo_made, o_copied)[k], B * UNITS)
                else:
                    pe.wait_ge(consumed, b * ITEMS + k - PBANKS + 1)
                pe.wait_ge(part_lo_made, b * ITEMS + k + 1)
                o_hi, o_lo = ring(k)
                w_hi_, w_lo_ = wo_parts(m)
                for c in range(HC):
                    if first and g == 0:
                        if m in SUMMED:
                            pe.wait_ge(*wo_lo_count(SUMMED.index(m), c))
                        else:
                            pe.wait_ge(wo_early_lo, ORDER.index(m) * HC + c + 1)
                    last = product(banks[:, k % PBANKS, :], (o_hi[:, c, :], o_lo[:, c, :]),
                                   (w_hi_[:, c, :], w_lo_[:, c, :]), c == 0, c == HC - 1)
                last.then_inc(product_done, 1)

            all_batches(pe, [(q_first, 0), (scores, SCORES_LAG), (q_second, 0), (values, VALUES_LAG),
                             (transpose_p, TRANSPOSE_LAG)], lambda j: out_product(0, j))
            all_batches(pe, [(lambda b, k: None if isinstance(b, int) and b == 0 and k < 3 else out_product(b, k), 0)],
                        count=ITEMS)


def kernel(x, ctx_2048, mask_BxS2_bf1, L0_xattn_Wq, L0_xattn_Wk, L0_xattn_Wv, L0_xattn_Wo,
           L0_xattn_ln_gamma, L0_xattn_ln_beta, L0_xattn_gate):
    import numpy as np
    import concourse.bacc as bacc
    from concourse.bass_utils import run_bass_kernel_spmd

    x = np.asarray(x)
    b, t, d = x.shape

    def laid(a):
        return np.ascontiguousarray(a)

    arrays = {
        "x": laid(x.reshape(b * t, d)),
        "x_t": laid(x.transpose(0, 2, 1).reshape(b * d, t)),
        "ctx_x": laid(np.asarray(ctx_2048).reshape(-1, d)),
        "mask": laid(np.asarray(mask_BxS2_bf1)),
        "wq_t": laid(np.asarray(L0_xattn_Wq).T),
        "wk_t": laid(np.asarray(L0_xattn_Wk).T),
        "wv_t": laid(np.asarray(L0_xattn_Wv).T),
        "wo_t": laid(np.asarray(L0_xattn_Wo).T),
        "gamma": laid(np.asarray(L0_xattn_ln_gamma).reshape(-1, P).T),
        "beta": laid(np.asarray(L0_xattn_ln_beta).reshape(-1, P).T),
        "gate": laid(np.asarray(L0_xattn_gate)),
    }
    nc = bacc.Bacc("TRN2", target_bir_lowering=False, num_devices=1)
    args = [nc.dram_tensor(name, a.shape, mybir.dt.from_np(a.dtype), kind="ExternalInput").ap()
            for name, a in arrays.items()]
    out = nc.dram_tensor("out", (b * t, d), F32, kind="ExternalOutput").ap()
    xattn_kernel(nc, *args, out)
    r = run_bass_kernel_spmd(nc, [arrays], core_ids=[0])
    return r.results[0]["out"].reshape(b, t, d)
```
